# Optimizing a Trainium2 kernel written in Bass

```python
import numpy as np
import jax
import jax.numpy as jnp

def _softmax(x, axis=-1):
    return jax.nn.softmax(x, axis=axis)

def _gelu(x):
    return jax.nn.gelu(x, approximate=True)

def _silu(x):
    return jax.nn.silu(x)

def _sigmoid(x):
    return jax.nn.sigmoid(x)

def _layernorm(x, axis=-1, eps=1e-05):
    m = jnp.mean(x, axis=axis, keepdims=True)
    v = jnp.var(x, axis=axis, keepdims=True)
    return (x - m) / jnp.sqrt(v + eps)

def _scatter_add(tgt, idx, src, axis=0):
    return tgt.at[idx].add(src)

def _segment_sum(src, seg, n):
    return jax.ops.segment_sum(src, seg, n)
kernel_name = 'mk_rec_standalone_d1_rec_r8_158dec'

def setup_inputs(seed: int=0):
    np.random.seed(seed)
    _w = jnp.asarray

    def _rec_inputs():
        import jax
        import jax.numpy as jnp
        _rk = jax.random.key(seed)
        r_items = jax.random.randint(jax.random.fold_in(_rk, 1), (2048,), 72, 99964, jnp.int32)
        r_users = jax.random.randint(jax.random.fold_in(_rk, 2), (2048,), 202, 499889, jnp.int32)
        r_history_users = jnp.stack([jax.random.randint(jax.random.fold_in(jax.random.fold_in(_rk, 3), 0), (2048,), 160, 499921, jnp.int32), jax.random.randint(jax.random.fold_in(jax.random.fold_in(_rk, 3), 1), (2048,), 19, 499891, jnp.int32), jax.random.randint(jax.random.fold_in(jax.random.fold_in(_rk, 3), 2), (2048,), 168, 499845, jnp.int32), jax.random.randint(jax.random.fold_in(jax.random.fold_in(_rk, 3), 3), (2048,), 72, 62493, jnp.int32), jax.random.randint(jax.random.fold_in(jax.random.fold_in(_rk, 3), 4), (2048,), 170, 499705, jnp.int32), jax.random.randint(jax.random.fold_in(jax.random.fold_in(_rk, 3), 5), (2048,), 134, 499997, jnp.int32), jax.random.randint(jax.random.fold_in(jax.random.fold_in(_rk, 3), 6), (2048,), 238, 499951, jnp.int32), jax.random.randint(jax.random.fold_in(jax.random.fold_in(_rk, 3), 7), (2048,), 10, 62498, jnp.int32), jax.random.randint(jax.random.fold_in(jax.random.fold_in(_rk, 3), 8), (2048,), 17, 499937, jnp.int32), jax.random.randint(jax.random.fold_in(jax.random.fold_in(_rk, 3), 9), (2048,), 115, 499916, jnp.int32), jax.random.randint(jax.random.fold_in(jax.random.fold_in(_rk, 3), 10), (2048,), 53, 499815, jnp.int32), jax.random.randint(jax.random.fold_in(jax.random.fold_in(_rk, 3), 11), (2048,), 99, 499978, jnp.int32), jax.random.randint(jax.random.fold_in(jax.random.fold_in(_rk, 3), 12), (2048,), 31, 499838, jnp.int32), jax.random.randint(jax.random.fold_in(jax.random.fold_in(_rk, 3), 13), (2048,), 32, 499929, jnp.int32), jax.random.randint(jax.random.fold_in(jax.random.fold_in(_rk, 3), 14), (2048,), 36, 499830, jnp.int32), jax.random.randint(jax.random.fold_in(jax.random.fold_in(_rk, 3), 15), (2048,), 75, 499843, jnp.int32), jax.random.randint(jax.random.fold_in(jax.random.fold_in(_rk, 3), 16), (2048,), 70, 499867, jnp.int32), jax.random.randint(jax.random.fold_in(jax.random.fold_in(_rk, 3), 17), (2048,), 305, 499902, jnp.int32), jax.random.randint(jax.random.fold_in(jax.random.fold_in(_rk, 3), 18), (2048,), 59, 499846, jnp.int32), jax.random.randint(jax.random.fold_in(jax.random.fold_in(_rk, 3), 19), (2048,), 3, 62456, jnp.int32), jax.random.randint(jax.random.fold_in(jax.random.fold_in(_rk, 3), 20), (2048,), 325, 499879, jnp.int32), jax.random.randint(jax.random.fold_in(jax.random.fold_in(_rk, 3), 21), (2048,), 53, 499841, jnp.int32), jax.random.randint(jax.random.fold_in(jax.random.fold_in(_rk, 3), 22), (2048,), 125, 499977, jnp.int32), jax.random.randint(jax.random.fold_in(jax.random.fold_in(_rk, 3), 23), (2048,), 224, 62451, jnp.int32), jax.random.randint(jax.random.fold_in(jax.random.fold_in(_rk, 3), 24), (2048,), 320, 499637, jnp.int32), jax.random.randint(jax.random.fold_in(jax.random.fold_in(_rk, 3), 25), (2048,), 1, 499932, jnp.int32), jax.random.randint(jax.random.fold_in(jax.random.fold_in(_rk, 3), 26), (2048,), 90, 499882, jnp.int32), jax.random.randint(jax.random.fold_in(jax.random.fold_in(_rk, 3), 27), (2048,), 86, 499915, jnp.int32), jax.random.randint(jax.random.fold_in(jax.random.fold_in(_rk, 3), 28), (2048,), 62, 499940, jnp.int32), jax.random.randint(jax.random.fold_in(jax.random.fold_in(_rk, 3), 29), (2048,), 18, 499965, jnp.int32), jax.random.randint(jax.random.fold_in(jax.random.fold_in(_rk, 3), 30), (2048,), 128, 499966, jnp.int32), jax.random.randint(jax.random.fold_in(jax.random.fold_in(_rk, 3), 31), (2048,), 36, 499690, jnp.int32), jax.random.randint(jax.random.fold_in(jax.random.fold_in(_rk, 3), 32), (2048,), 92, 62495, jnp.int32), jax.random.randint(jax.random.fold_in(jax.random.fold_in(_rk, 3), 33), (2048,), 247, 499771, jnp.int32), jax.random.randint(jax.random.fold_in(jax.random.fold_in(_rk, 3), 34), (2048,), 77, 499954, jnp.int32), jax.random.randint(jax.random.fold_in(jax.random.fold_in(_rk, 3), 35), (2048,), 253, 499908, jnp.int32), jax.random.randint(jax.random.fold_in(jax.random.fold_in(_rk, 3), 36), (2048,), 45, 499651, jnp.int32), jax.random.randint(jax.random.fold_in(jax.random.fold_in(_rk, 3), 37), (2048,), 303, 499854, jnp.int32), jax.random.randint(jax.random.fold_in(jax.random.fold_in(_rk, 3), 38), (2048,), 146, 499980, jnp.int32), jax.random.randint(jax.random.fold_in(jax.random.fold_in(_rk, 3), 39), (2048,), 559, 62460, jnp.int32), jax.random.randint(jax.random.fold_in(jax.random.fold_in(_rk, 3), 40), (2048,), 101, 62471, jnp.int32), jax.random.randint(jax.random.fold_in(jax.random.fold_in(_rk, 3), 41), (2048,), 184, 499862, jnp.int32), jax.random.randint(jax.random.fold_in(jax.random.fold_in(_rk, 3), 42), (2048,), 68, 499997, jnp.int32), jax.random.randint(jax.random.fold_in(jax.random.fold_in(_rk, 3), 43), (2048,), 107, 499970, jnp.int32), jax.random.randint(jax.random.fold_in(jax.random.fold_in(_rk, 3), 44), (2048,), 17, 499893, jnp.int32), jax.random.randint(jax.random.fold_in(jax.random.fold_in(_rk, 3), 45), (2048,), 384, 499387, jnp.int32), jax.random.randint(jax.random.fold_in(jax.random.fold_in(_rk, 3), 46), (2048,), 113, 499743, jnp.int32), jax.random.randint(jax.random.fold_in(jax.random.fold_in(_rk, 3), 47), (2048,), 497, 499855, jnp.int32), jax.random.randint(jax.random.fold_in(jax.random.fold_in(_rk, 3), 48), (2048,), 50, 499761, jnp.int32), jax.random.randint(jax.random.fold_in(jax.random.fold_in(_rk, 3), 49), (2048,), 11, 499910, jnp.int32), jax.random.randint(jax.random.fold_in(jax.random.fold_in(_rk, 3), 50), (2048,), 71, 499946, jnp.int32), jax.random.randint(jax.random.fold_in(jax.random.fold_in(_rk, 3), 51), (2048,), 14, 499970, jnp.int32), jax.random.randint(jax.random.fold_in(jax.random.fold_in(_rk, 3), 52), (2048,), 38, 499931, jnp.int32), jax.random.randint(jax.random.fold_in(jax.random.fold_in(_rk, 3), 53), (2048,), 136, 499836, jnp.int32), jax.random.randint(jax.random.fold_in(jax.random.fold_in(_rk, 3), 54), (2048,), 39, 499868, jnp.int32), jax.random.randint(jax.random.fold_in(jax.random.fold_in(_rk, 3), 55), (2048,), 233, 499989, jnp.int32), jax.random.randint(jax.random.fold_in(jax.random.fold_in(_rk, 3), 56), (2048,), 66, 499854, jnp.int32), jax.random.randint(jax.random.fold_in(jax.random.fold_in(_rk, 3), 57), (2048,), 34, 499969, jnp.int32), jax.random.randint(jax.random.fold_in(jax.random.fold_in(_rk, 3), 58), (2048,), 17, 62496, jnp.int32), jax.random.randint(jax.random.fold_in(jax.random.fold_in(_rk, 3), 59), (2048,), 459, 499807, jnp.int32), jax.random.randint(jax.random.fold_in(jax.random.fold_in(_rk, 3), 60), (2048,), 11, 62498, jnp.int32), jax.random.randint(jax.random.fold_in(jax.random.fold_in(_rk, 3), 61), (2048,), 4, 499901, jnp.int32), jax.random.randint(jax.random.fold_in(jax.random.fold_in(_rk, 3), 62), (2048,), 41, 499899, jnp.int32), jax.random.randint(jax.random.fold_in(jax.random.fold_in(_rk, 3), 63), (2048,), 153, 499995, jnp.int32), jax.random.randint(jax.random.fold_in(jax.random.fold_in(_rk, 3), 64), (2048,), 68, 499908, jnp.int32), jax.random.randint(jax.random.fold_in(jax.random.fold_in(_rk, 3), 65), (2048,), 138, 499947, jnp.int32), jax.random.randint(jax.random.fold_in(jax.random.fold_in(_rk, 3), 66), (2048,), 23, 62494, jnp.int32), jax.random.randint(jax.random.fold_in(jax.random.fold_in(_rk, 3), 67), (2048,), 91, 62495, jnp.int32), jax.random.randint(jax.random.fold_in(jax.random.fold_in(_rk, 3), 68), (2048,), 43, 499807, jnp.int32), jax.random.randint(jax.random.fold_in(jax.random.fold_in(_rk, 3), 69), (2048,), 30, 499942, jnp.int32), jax.random.randint(jax.random.fold_in(jax.random.fold_in(_rk, 3), 70), (2048,), 18, 499964, jnp.int32), jax.random.randint(jax.random.fold_in(jax.random.fold_in(_rk, 3), 71), (2048,), 2, 499926, jnp.int32), jax.random.randint(jax.random.fold_in(jax.random.fold_in(_rk, 3), 72), (2048,), 29, 499971, jnp.int32), jax.random.randint(jax.random.fold_in(jax.random.fold_in(_rk, 3), 73), (2048,), 143, 499701, jnp.int32), jax.random.randint(jax.random.fold_in(jax.random.fold_in(_rk, 3), 74), (2048,), 7, 499981, jnp.int32), jax.random.randint(jax.random.fold_in(jax.random.fold_in(_rk, 3), 75), (2048,), 82, 62482, jnp.int32), jax.random.randint(jax.random.fold_in(jax.random.fold_in(_rk, 3), 76), (2048,), 30, 499674, jnp.int32), jax.random.randint(jax.random.fold_in(jax.random.fold_in(_rk, 3), 77), (2048,), 63, 499931, jnp.int32), jax.random.randint(jax.random.fold_in(jax.random.fold_in(_rk, 3), 78), (2048,), 135, 499949, jnp.int32), jax.random.randint(jax.random.fold_in(jax.random.fold_in(_rk, 3), 79), (2048,), 313, 62499, jnp.int32), jax.random.randint(jax.random.fold_in(jax.random.fold_in(_rk, 3), 80), (2048,), 286, 499854, jnp.int32), jax.random.randint(jax.random.fold_in(jax.random.fold_in(_rk, 3), 81), (2048,), 17, 499994, jnp.int32), jax.random.randint(jax.random.fold_in(jax.random.fold_in(_rk, 3), 82), (2048,), 14, 499967, jnp.int32), jax.random.randint(jax.random.fold_in(jax.random.fold_in(_rk, 3), 83), (2048,), 16, 499931, jnp.int32), jax.random.randint(jax.random.fold_in(jax.random.fold_in(_rk, 3), 84), (2048,), 59, 499907, jnp.int32), jax.random.randint(jax.random.fold_in(jax.random.fold_in(_rk, 3), 85), (2048,), 458, 499979, jnp.int32), jax.random.randint(jax.random.fold_in(jax.random.fold_in(_rk, 3), 86), (2048,), 75, 499939, jnp.int32), jax.random.randint(jax.random.fold_in(jax.random.fold_in(_rk, 3), 87), (2048,), 61, 499963, jnp.int32), jax.random.randint(jax.random.fold_in(jax.random.fold_in(_rk, 3), 88), (2048,), 269, 62489, jnp.int32), jax.random.randint(jax.random.fold_in(jax.random.fold_in(_rk, 3), 89), (2048,), 80, 62496, jnp.int32), jax.random.randint(jax.random.fold_in(jax.random.fold_in(_rk, 3), 90), (2048,), 11, 62476, jnp.int32), jax.random.randint(jax.random.fold_in(jax.random.fold_in(_rk, 3), 91), (2048,), 196, 499958, jnp.int32), jax.random.randint(jax.random.fold_in(jax.random.fold_in(_rk, 3), 92), (2048,), 23, 499930, jnp.int32), jax.random.randint(jax.random.fold_in(jax.random.fold_in(_rk, 3), 93), (2048,), 295, 499626, jnp.int32), jax.random.randint(jax.random.fold_in(jax.random.fold_in(_rk, 3), 94), (2048,), 97, 499934, jnp.int32), jax.random.randint(jax.random.fold_in(jax.random.fold_in(_rk, 3), 95), (2048,), 157, 499937, jnp.int32), jax.random.randint(jax.random.fold_in(jax.random.fold_in(_rk, 3), 96), (2048,), 24, 499978, jnp.int32), jax.random.randint(jax.random.fold_in(jax.random.fold_in(_rk, 3), 97), (2048,), 124, 499977, jnp.int32), jax.random.randint(jax.random.fold_in(jax.random.fold_in(_rk, 3), 98), (2048,), 71, 499858, jnp.int32), jax.random.randint(jax.random.fold_in(jax.random.fold_in(_rk, 3), 99), (2048,), 124, 499967, jnp.int32)], axis=1)
        return (r_items, r_users, r_history_users)
    r_items, r_users, r_history_users = _rec_inputs()

    def _L0_rec_setup():
        import jax, jax.numpy as jnp
        import numpy as np
        B, H, D = (512, 100, 128)
        N_ITEM, M_USER = (12500, 62500)
        D_IN, D1, D2 = (3 * D, 1024, 512)
        DICE_EPS = 0.001
        BN_EPS = 1e-05

        def _xavier(key, shape):
            fan_in, fan_out = (shape[0], shape[1])
            lim = jnp.sqrt(6.0 / (fan_in + fan_out))
            return jax.random.uniform(key, shape, jnp.float32, -lim, lim)

        def _dice(x, alpha):
            avg = x.mean(axis=1, keepdims=True)
            var = jnp.sum((x - avg) ** 2 + DICE_EPS, axis=1, keepdims=True)
            ps = jax.nn.sigmoid((x - avg) / jnp.sqrt(var))
            return ps * x + (1.0 - ps) * alpha * x

        def _batchnorm(x, gamma, beta):
            mu = x.mean(axis=0, keepdims=True)
            var = x.var(axis=0, keepdims=True)
            return (x - mu) / jnp.sqrt(var + BN_EPS) * gamma + beta
        key = jax.random.key(seed)
        ks = jax.random.split(key, 12)
        return {'items': jax.random.randint(ks[0], (B,), 0, N_ITEM), 'users': jax.random.randint(ks[1], (B,), 0, M_USER), 'history_users': jax.random.randint(ks[2], (B, H), 0, M_USER), 'item_table': _xavier(ks[3], (N_ITEM, D)), 'user_table': _xavier(ks[4], (M_USER, D)), 'W1': _xavier(ks[5], (D_IN, D1)), 'b1': jnp.zeros((D1,), jnp.float32), 'g1': jnp.ones((D1,), jnp.float32), 'be1': jnp.zeros((D1,), jnp.float32), 'a1': jax.random.normal(ks[6], (1,), jnp.float32), 'W2': _xavier(ks[7], (D1, D2)), 'b2': jnp.zeros((D2,), jnp.float32), 'g2': jnp.ones((D2,), jnp.float32), 'be2': jnp.zeros((D2,), jnp.float32), 'a2': jax.random.normal(ks[8], (1,), jnp.float32), 'W3': _xavier(ks[9], (D2, 1)), 'b3': jnp.zeros((1,), jnp.float32)}
    _L0_rec_all = _L0_rec_setup()
    _L0_rec_in = {k: v for k, v in _L0_rec_all.items() if k in ('item_table', 'user_table', 'W1', 'b1', 'g1', 'be1', 'a1', 'W2', 'b2', 'g2', 'be2', 'a2', 'W3', 'b3')}
    del _L0_rec_all
    return {'r_items': r_items, 'r_users': r_users, 'r_history_users': r_history_users, 'L0_rec_item_table': _L0_rec_in['item_table'], 'L0_rec_user_table': _L0_rec_in['user_table'], 'L0_rec_W1': _L0_rec_in['W1'], 'L0_rec_b1': _L0_rec_in['b1'], 'L0_rec_g1': _L0_rec_in['g1'], 'L0_rec_be1': _L0_rec_in['be1'], 'L0_rec_a1': _L0_rec_in['a1'], 'L0_rec_W2': _L0_rec_in['W2'], 'L0_rec_b2': _L0_rec_in['b2'], 'L0_rec_g2': _L0_rec_in['g2'], 'L0_rec_be2': _L0_rec_in['be2'], 'L0_rec_a2': _L0_rec_in['a2'], 'L0_rec_W3': _L0_rec_in['W3'], 'L0_rec_b3': _L0_rec_in['b3']}

def reference(r_items, r_users, r_history_users, L0_rec_item_table, L0_rec_user_table, L0_rec_W1, L0_rec_b1, L0_rec_g1, L0_rec_be1, L0_rec_a1, L0_rec_W2, L0_rec_b2, L0_rec_g2, L0_rec_be2, L0_rec_a2, L0_rec_W3, L0_rec_b3):
    import jax
    import jax.numpy as jnp

    def _L0_rec_ref(items, users, history_users, item_table, user_table, W1, b1, g1, be1, a1, W2, b2, g2, be2, a2, W3, b3):
        import jax, jax.numpy as jnp
        import numpy as np
        B, H, D = (512, 100, 128)
        N_ITEM, M_USER = (12500, 62500)
        D_IN, D1, D2 = (3 * D, 1024, 512)
        DICE_EPS = 0.001
        BN_EPS = 1e-05

        def _xavier(key, shape):
            fan_in, fan_out = (shape[0], shape[1])
            lim = jnp.sqrt(6.0 / (fan_in + fan_out))
            return jax.random.uniform(key, shape, jnp.float32, -lim, lim)

        def _dice(x, alpha):
            avg = x.mean(axis=1, keepdims=True)
            var = jnp.sum((x - avg) ** 2 + DICE_EPS, axis=1, keepdims=True)
            ps = jax.nn.sigmoid((x - avg) / jnp.sqrt(var))
            return ps * x + (1.0 - ps) * alpha * x

        def _batchnorm(x, gamma, beta):
            mu = x.mean(axis=0, keepdims=True)
            var = x.var(axis=0, keepdims=True)
            return (x - mu) / jnp.sqrt(var + BN_EPS) * gamma + beta
        items_emb = item_table[items]
        user_emb = user_table[users]
        hist_emb = user_table[history_users]
        scores = jnp.einsum('bhd,bd->bh', hist_emb, user_emb)
        user_his_emb = jnp.einsum('bh,bhd->bd', scores, hist_emb)
        x = jnp.concatenate([items_emb, user_his_emb, user_emb], axis=1)
        x = _dice(_batchnorm(x @ W1 + b1, g1, be1), a1)
        x = _dice(_batchnorm(x @ W2 + b2, g2, be2), a2)
        return x @ W3 + b3
    y = _L0_rec_ref(r_items, r_users, r_history_users, L0_rec_item_table, L0_rec_user_table, L0_rec_W1, L0_rec_b1, L0_rec_g1, L0_rec_be1, L0_rec_a1, L0_rec_W2, L0_rec_b2, L0_rec_g2, L0_rec_be2, L0_rec_a2, L0_rec_W3, L0_rec_b3)
    return y

_drawn_inputs = setup_inputs


def setup_inputs(seed=0):
    import zlib

    import numpy as np

    out = dict(_drawn_inputs(seed))
    spreads = {'L0_rec_b1': (0.0, 0.8),
     'L0_rec_g1': (1.0, 0.2),
     'L0_rec_be1': (0.0, 0.8),
     'L0_rec_b2': (0.0, 0.8),
     'L0_rec_g2': (1.0, 0.2),
     'L0_rec_be2': (0.0, 0.323)}
    factors = {}
    for name, (base, spread) in spreads.items():
        noise = np.random.default_rng([zlib.crc32(name.encode()), seed]).standard_normal(out[name].shape)
        drawn = base * np.exp(spread * noise) if base else spread * noise
        out[name] = jnp.asarray(drawn.astype(out[name].dtype))
    for name, factor in factors.items():
        out[name] = (out[name] * factor).astype(out[name].dtype)
    return out
```

```python
from contextlib import ExitStack

import concourse.bass as bass
from concourse import mybir


P = 128
F32 = mybir.dt.float32
I32 = mybir.dt.int32
ALU = mybir.AluOpType
ACT = mybir.ActivationFunctionType
AX_X = mybir.AxisListType.X

GROUP = 8
HALF = GROUP // 2
MIN_GROUPS = 2
DICE_EPS = 0.001
BN_EPS = 1e-05
CHUNK = 256
USED = -1.0e9


def recommender_kernel(nc, items, users, history, item_table, user_table, W1, b1, g1, be1, a1,
                       W2, b2, g2, be2, a2, W3, b3, out):
    B, HIST = history.shape
    N_ITEM, D = item_table.shape
    N_USER = user_table.shape[0]
    D_IN, D1 = W1.shape
    D2 = W2.shape[1]
    TILES = B // P
    KX, M1, M2 = D_IN // P, D1 // P, D2 // P
    CHUNKS = B // CHUNK
    ROUNDS = -(-HIST // GROUP)
    KEYS = ROUNDS * GROUP
    LAST = N_USER - 1
    assert D == P and D_IN == 3 * P and B % CHUNK == 0 and TILES * P == B and CHUNKS % 2 == 0

    with ExitStack() as ctx:
        def sb(name, shape, dt=F32):
            return ctx.enter_context(nc.sbuf_tensor(name, shape, dt))

        def sem(name):
            return ctx.enter_context(nc.semaphore(name))

        h1 = sb("h1", [P, M1, B])
        w1 = sb("w1", [P, KX, D1])
        w2 = sb("w2", [P, M1, D2])
        wide = sb("wide", [P, 4 * B])
        user_rows = wide[:, 0:B].rearrange("p (t d) -> p t d", d=D)
        item_rows = wide[:, B:2 * B].rearrange("p (t d) -> p t d", d=D)
        user_T = wide[:, 2 * B:3 * B]
        item_T = wide[:, 3 * B:4 * B]
        h2 = wide[:, 0:M2 * B].rearrange("p (m b) -> p m b", m=M2)
        work = sb("work", [P, 3 * M1 * CHUNK])
        n_idx = TILES * HIST
        hist_raw = work[:, 0:n_idx].bitcast(I32)
        hist_fix = work[:, n_idx:2 * n_idx]
        keys = work[:, 2 * n_idx:2 * n_idx + (TILES + 1) * KEYS].rearrange("p (t k) -> p t k", k=KEYS)
        assert 2 * n_idx + (TILES + 1) * KEYS <= 3 * M1 * CHUNK
        dev = [work[:, i * M1 * CHUNK:(i + 1) * M1 * CHUNK] for i in range(2)]
        dev_sq = work[:, 2 * M1 * CHUNK:3 * M1 * CHUNK]

        ids_raw = sb("ids_raw", [2 * TILES, P], I32)
        ids_f = sb("ids_f", [2 * TILES, P])
        ids_neg = sb("ids_neg", [P, 2 * TILES])
        ids_fix = sb("ids_fix", [P, 2 * TILES])
        ids = sb("ids", [P, 2 * TILES], I32)
        counts = sb("counts", [P, TILES])
        fullest = sb("fullest", [TILES, 1])
        fullest_row = sb("fullest_row", [TILES, P])
        more = sb("more", [P, TILES, ROUNDS])
        groups = sb("groups", [P, TILES])
        groups2 = sb("groups2", [P, TILES])
        ones_t = sb("ones_t", [P, TILES])
        ends_f = sb("ends_f", [P, TILES])
        ends = sb("ends", [P, TILES + 1], I32)
        left = sb("left", [P, TILES])
        tile_keys = sb("tile_keys", [P, KEYS])
        top = sb("top", [P, GROUP])
        slot_idx = sb("slot_idx", [P, GROUP], I32)
        rows = sb("rows", [P, GROUP, D])
        prod = sb("prod", [P, GROUP, D])
        score = sb("score", [P, GROUP])
        scaled = sb("scaled", [P, GROUP, D])
        last_row = sb("last_row", [P, D])
        last_prod = sb("last_prod", [P, D])
        last_score = sb("last_score", [P, 1])
        last_weight = sb("last_weight", [P, 1])
        last_scaled = sb("last_scaled", [P, D])
        pooled_T = sb("pooled_T", [P, P])
        ident = sb("ident", [P, P])
        mean_of1 = sb("mean_of1", [P, P])
        mean_of2 = sb("mean_of2", [P, P])
        ones = sb("ones", [P, P])
        n_par = 3 * M1 + 4 * M2
        par_rows = sb("par_rows", [n_par, P])
        par = sb("par", [P, n_par])
        alphas = sb("alphas", [P, 2])
        rest = sb("rest", [P, 2])
        bias3 = sb("bias3", [1, 1])
        stats1 = sb("stats1", [P, M1, TILES, 6])
        stats2 = sb("stats2", [P, M2, CHUNKS, 6])
        mv = sb("mv", [P, M1, 2])
        bn_v = sb("bn_v", [P, M1])
        bn_s = sb("bn_s", [P, M1])
        bn_r = sb("bn_r", [P, M1])
        bn_m = sb("bn_m", [P, M1])
        scale = [sb(f"scale{n}", [P, M1]) for n in (1, 2)]
        shift = [sb(f"shift{n}", [P, M1]) for n in (1, 2)]
        col_sum = sb("col_sum", [P, CHUNK])
        sq_sum = sb("sq_sum", [P, CHUNK])
        var_eps = sb("var_eps", [P, CHUNK])
        root = sb("root", [P, CHUNK])
        inv = sb("inv", [P, CHUNK])
        y_row = sb("y_row", [1, B])
        b1c, g1c, be1c = (par[:, i * M1:(i + 1) * M1] for i in range(3))
        b2c, g2c, be2c, w3c = (par[:, 3 * M1 + i * M2:3 * M1 + (i + 1) * M2] for i in range(4))

        ps = ctx.enter_context(nc.psum_tensor("ps", [P, 8, 512], F32))
        ids_ps = ps[:, 0, 0:2 * TILES]
        counts_ps = ps[0:TILES, 0, 64:64 + P]
        fullest_ps = ps[:, 0, 192:192 + TILES]
        par_ps = ps[:, 7, 0:n_par]
        pooled_ps = ps[:, 1, 0:P]
        l1_ps = ps[:, 2:4, :].rearrange("p a (m b) -> p (a m) b", b=P)
        user_now = ps[:, 4, 0:D]
        turn_ps = [ps[:, 5 + i, :] for i in range(2)]
        l2_ps = [ps[:, 2 * i:2 * i + 2, :].rearrange("p a (m b) -> p (a m) b", b=CHUNK) for i in range(2)]
        avg_ps = ps[:, 4, 0:CHUNK]
        var_ps = ps[:, 5, 0:CHUNK]
        y_ps = [ps[0:1, 6 + i, 0:CHUNK] for i in range(2)]

        ids_loaded = sem("ids_loaded")
        hist_loaded = sem("hist_loaded")
        par_loaded = sem("par_loaded")
        alphas_loaded = sem("alphas_loaded")
        last_loaded = sem("last_loaded")
        w1_loaded = sem("w1_loaded")
        w2_loaded = sem("w2_loaded")
        consts_made = sem("consts_made")
        ids_turned = sem("ids_turned")
        prep = sem("prep")
        ids_float = sem("ids_float")
        ids_ready = sem("ids_ready")
        counts_ready = sem("counts_ready")
        counts_turned = sem("counts_turned")
        fullest_ready = sem("fullest_ready")
        fullest_spread = sem("fullest_spread")
        plan_ready = sem("plan_ready")
        par_turned = sem("par_turned")
        par_ready = sem("par_ready")
        users_landed = sem("users_landed")
        items_landed = sem("items_landed")
        block_turned = sem("block_turned")
        block_kept = sem("block_kept")
        keys_loaded = sem("keys_loaded")
        top_found = sem("top_found")
        keys_cut = sem("keys_cut")
        idx_ready = sem("idx_ready")
        landed = [sem(f"landed{j}") for j in range(GROUP)]
        user_set = sem("user_set")
        last_dotted = sem("last_dotted")
        last_weighed = sem("last_weighed")
        last_ready = sem("last_ready")
        scored = sem("scored")
        slot_scaled = sem("slot_scaled")
        slot_summed = sem("slot_summed")
        pooled = sem("pooled")
        pooled_kept = sem("pooled_kept")
        l1_done = sem("l1_done")
        l1_kept = sem("l1_kept")
        stats_done = sem("stats_done")
        passed = sem("passed")
        aggregated = [sem(f"aggregated{n}") for n in (1, 2)]
        bn_rooted = [sem(f"bn_rooted{n}") for n in (1, 2)]
        bn_step = [sem(f"bn_step{n}") for n in (1, 2)]
        bn_ready = [sem(f"bn_ready{n}") for n in (1, 2)]
        normed_act = [sem(f"normed_act{n}") for n in (1, 2)]
        normed_pool = [sem(f"normed_pool{n}") for n in (1, 2)]
        col_summed = [sem(f"col_summed{n}") for n in (1, 2)]
        avg_ready = [sem(f"avg_ready{n}") for n in (1, 2)]
        dev_ready = [sem(f"dev_ready{n}") for n in (1, 2)]
        squared = [sem(f"squared{n}") for n in (1, 2)]
        sq_summed = [sem(f"sq_summed{n}") for n in (1, 2)]
        var_ready = [sem(f"var_ready{n}") for n in (1, 2)]
        var_kept = [sem(f"var_kept{n}") for n in (1, 2)]
        rooted = [sem(f"rooted{n}") for n in (1, 2)]
        inverted = [sem(f"inverted{n}") for n in (1, 2)]
        arg_ready = [sem(f"arg_ready{n}") for n in (1, 2)]
        gated = [sem(f"gated{n}") for n in (1, 2)]
        mixed = [sem(f"mixed{n}") for n in (1, 2)]
        dice_done = [sem(f"dice_done{n}") for n in (1, 2)]
        product_done = [sem(f"product_done{n}") for n in (1, 2)]
        l2_kept = sem("l2_kept")
        l2_stats_done = sem("l2_stats_done")
        y_kept = sem("y_kept")
        stored = sem("stored")

        N_CONSTS = 5

        def hold(eng, semaphore, value):
            if not isinstance(value, int):
                eng.wait_ge(semaphore, value)
                eng.sem_inc(passed, 1)
            elif value > 0:
                eng.wait_ge(semaphore, value)

        def span(eng, t):
            first = eng.value_load(ends[0:1, bass.ds(t, 1)], min_val=0, max_val=TILES * ROUNDS)
            end = eng.value_load(ends[0:1, bass.ds(t + 1, 1)], min_val=0, max_val=TILES * ROUNDS)
            return first, end

        def over_tiles(eng, tile):
            tile(0, 0)
            tile(1, 1)
            with eng.Fori(2, TILES) as t:
                tile(t, 2)

        def pipelined(eng, step):
            for i in range(CHUNKS + 4):
                step(i, i % 2, lambda lag, i=i: 0 <= i - lag < CHUNKS)

        def chunk(c):
            return bass.ds(c * CHUNK, CHUNK)

        block = ctx.enter_context(nc.Block())

        @block.sync
        def _(sp):
            sp.dma_start(ids_raw[0:TILES, :], users.rearrange("(t p) -> t p", p=P)).then_inc(ids_loaded, 16)
            sp.dma_start(ids_raw[TILES:2 * TILES, :], items.rearrange("(t p) -> t p", p=P)).then_inc(ids_loaded, 16)
            sp.dma_start(hist_raw.rearrange("p (t h) -> p t h", h=HIST),
                         history.rearrange("(t p) h -> p t h", p=P)).then_inc(hist_loaded, 16)
            sp.dma_start(last_row[:, :], user_table[LAST:LAST + 1, :].to_broadcast([P, D])).then_inc(last_loaded, 16)
            at = 0
            for v, m in ((b1, M1), (g1, M1), (be1, M1), (b2, M2), (g2, M2), (be2, M2)):
                sp.dma_start(par_rows[at:at + m, :], v.rearrange("(m p) -> m p", p=P)).then_inc(par_loaded, 16)
                at += m
            sp.dma_start(par_rows[at:at + M2, :], W3.rearrange("(m p) a -> m (p a)", p=P)).then_inc(par_loaded, 16)
            sp.dma_start(w1[:, :, :], W1.rearrange("(k p) n -> p k n", p=P)).then_inc(w1_loaded, 16)
            for i, a in enumerate((a1, a2)):
                sp.dma_start(alphas[:, i:i + 1], a.rearrange("(a b) -> a b", a=1).to_broadcast([P, 1])).then_inc(alphas_loaded, 16)
            sp.dma_start(bias3[:, :], b3.rearrange("(a b) -> a b", a=1)).then_inc(alphas_loaded, 16)
            sp.dma_start(w2[:, :, :], W2.rearrange("(k p) n -> p k n", p=P)).then_inc(w2_loaded, 16)
            sp.wait_ge(y_kept, CHUNKS)
            sp.dma_start(out.rearrange("b a -> a b"), y_row[:, :]).then_inc(stored, 16)
            sp.wait_ge(stored, 16)

        @block.gpsimd
        def _(pool):
            nc.gpsimd.memset(ident[:, :], 0.0).then_inc(consts_made, 1)
            nc.gpsimd.memset(ones[:, :], 1.0).then_inc(consts_made, 1)
            pool.wait_ge(consts_made, 2)
            nc.gpsimd.affine_select(out=ident[:, :], in_=ident[:, :], compare_op=ALU.not_equal, fill=1.0,
                                    base=0, pattern=[[-1, P]], channel_multiplier=1).then_inc(consts_made, 1)
            nc.gpsimd.memset(mean_of1[:, :], 1.0 / D1).then_inc(consts_made, 1)
            nc.gpsimd.memset(mean_of2[:, :], 1.0 / D2).then_inc(consts_made, 1)
            pool.wait_ge(ids_ready, 1)
            for t in range(TILES):
                nc.gpsimd.indirect_dma_start(user_rows[:, t, :], None, user_table,
                                             bass.IndirectOffsetOnAxis(ids[:, t:t + 1], 0)).then_inc(users_landed, 16)
            for t in range(TILES):
                nc.gpsimd.indirect_dma_start(item_rows[:, t, :], None, item_table,
                                             bass.IndirectOffsetOnAxis(ids[:, TILES + t:TILES + t + 1], 0)).then_inc(items_landed, 16)
            pool.wait_ge(plan_ready, 1)

            def tile(t, _):
                first, end = span(pool, t)
                with pool.Fori(first, end) as g:
                    for half in range(2):
                        hold(pool, idx_ready, 2 * g + half + 1)
                        for j in range(half * HALF, half * HALF + HALF):
                            hold(pool, slot_scaled, GROUP * g + j + 1)
                            nc.gpsimd.indirect_dma_start(
                                rows[:, j, :], None, user_table,
                                bass.IndirectOffsetOnAxis(slot_idx[:, j:j + 1], 0)).then_inc(landed[j], 16)

            with pool.Fori(0, TILES) as t:
                tile(t, 0)
            for n, (m, src) in enumerate(((M1, h1), (M2, h2))):
                pool.wait_ge(bn_ready[n], 1)

                def normalise(c):
                    for k in range(m // 2, m):
                        nc.gpsimd.tensor_scalar(src[:, k, chunk(c)], src[:, k, chunk(c)], scale[n][:, k:k + 1],
                                                shift[n][:, k:k + 1], ALU.mult, ALU.add).then_inc(normed_pool[n], 1)

                normalise(0)
                normalise(1)

                def step(i, odd, live):
                    if live(-2):
                        normalise(i + 2)
                    if live(1):
                        d = dev[1 - odd][:, 0:m * CHUNK]
                        hold(pool, gated[n], i)
                        nc.gpsimd.tensor_scalar(d, d, rest[:, n:n + 1], alphas[:, n:n + 1],
                                                ALU.mult, ALU.add).then_inc(mixed[n], 1)
                pipelined(pool, step)

        @block.vector
        def _(dve):
            dve.wait_ge(ids_loaded, 32)
            nc.vector.tensor_copy(ids_f[:, :], ids_raw[:, :]).then_inc(ids_float, 1)
            dve.wait_ge(ids_turned, 1)
            for i, n in ((0, N_USER), (1, N_ITEM)):
                c = slice(i * TILES, (i + 1) * TILES)
                nc.vector.tensor_scalar(ids_neg[:, c], ids_ps[:, c], 0.0, float(n), ALU.is_lt, ALU.mult).then_inc(prep, 1)
            dve.wait_ge(prep, 2)
            nc.vector.tensor_tensor(ids_fix[:, :], ids_ps, ids_neg[:, :], ALU.add).then_inc(prep, 1)
            dve.wait_ge(prep, 3)
            for i, n in ((0, N_USER), (1, N_ITEM)):
                c = slice(i * TILES, (i + 1) * TILES)
                last = nc.vector.tensor_scalar(ids[:, c], ids_fix[:, c], 0.0, float(n - 1), ALU.max, ALU.min)
                last.then_inc(prep, 1)
            dve.wait_ge(prep, 5)
            dve.sem_inc(ids_ready, 1)
            dve.wait_ge(hist_loaded, 16)
            nc.vector.tensor_scalar(hist_fix, hist_raw, 0.0, float(N_USER), ALU.is_lt, ALU.mult).then_inc(prep, 1)
            nc.vector.memset(keys[:, 0:TILES, HIST:KEYS], -float(LAST)).then_inc(prep, 1)
            nc.vector.memset(keys[:, TILES, :], 0.0).then_inc(prep, 1)
            nc.vector.memset(ones_t[:, :], 1.0).then_inc(prep, 1)
            nc.vector.memset(ends[:, 0:1], 0).then_inc(prep, 1)
            dve.wait_ge(prep, 10)
            nc.vector.tensor_tensor(hist_fix, hist_raw, hist_fix, ALU.add).then_inc(prep, 1)
            dve.wait_ge(prep, 11)
            nc.vector.tensor_scalar(hist_fix, hist_fix, -1.0, 0.0, ALU.mult, ALU.min).then_inc(prep, 1)
            dve.wait_ge(prep, 12)
            own = keys[:, 0:TILES, 0:HIST]
            nc.vector.tensor_scalar(own, hist_fix.rearrange("p (t h) -> p t h", h=HIST), -float(LAST), None,
                                    ALU.max).then_inc(prep, 1)
            dve.wait_ge(prep, 13)
            below = hist_fix.rearrange("p (t h) -> p t h", h=HIST)
            nc.vector.tensor_scalar(below, own, -float(LAST), None, ALU.is_gt).then_inc(prep, 1)
            dve.wait_ge(prep, 14)
            nc.vector.tensor_reduce(counts[:, :], below, AX_X, ALU.add).then_inc(counts_ready, 1)
            dve.wait_ge(counts_turned, 1)
            nc.vector.tensor_reduce(fullest[:, :], counts_ps, AX_X, ALU.max).then_inc(prep, 1)
            dve.wait_ge(prep, 15)
            dve.wait_ge(consts_made, N_CONSTS)
            nc.vector.tensor_scalar(fullest_row[:, :], ones[0:TILES, :], fullest[:, 0:1], None, ALU.mult).then_inc(fullest_ready, 1)
            dve.wait_ge(fullest_spread, 1)
            for r in range(ROUNDS):
                nc.vector.tensor_scalar(more[:, :, r], fullest_ps, float(r * GROUP), None, ALU.is_gt).then_inc(prep, 1)
            dve.wait_ge(prep, 15 + ROUNDS)
            nc.vector.tensor_reduce(groups[:, :], more[:, :, :], AX_X, ALU.add).then_inc(prep, 1)
            dve.wait_ge(prep, 16 + ROUNDS)
            nc.vector.tensor_scalar(groups2[:, :], groups[:, :], float(MIN_GROUPS), None, ALU.max).then_inc(prep, 1)
            dve.wait_ge(prep, 17 + ROUNDS)
            nc.vector.tensor_scalar(left[:, :], groups2[:, :], -float(GROUP), float(HIST), ALU.mult, ALU.add).then_inc(prep, 1)
            nc.vector.tensor_tensor_scan(ends_f[:, :], ones_t[:, :], groups2[:, :], 0.0, ALU.mult, ALU.add).then_inc(prep, 1)
            dve.wait_ge(prep, 19 + ROUNDS)
            nc.vector.tensor_copy(ends[:, 1:TILES + 1], ends_f[:, :]).then_inc(prep, 1)
            dve.wait_ge(prep, 20 + ROUNDS)
            dve.sem_inc(plan_ready, 1)

            def load_keys(t, times):
                hold(dve, keys_cut, times)
                nc.vector.tensor_copy(tile_keys[:, :], keys[:, t, :]).then_inc(keys_loaded, 1)

            def find(n):
                hold(dve, keys_cut, n)
                hold(dve, idx_ready, 2 * n)
                nc.vector.max(top[:, :], tile_keys[:, :]).then_inc(top_found, 1)
                hold(dve, top_found, n + 1)
                nc.vector.match_replace(tile_keys[:, :], top[:, :], tile_keys[:, :], USED).then_inc(keys_cut, 1)

            def hand(n, half):
                c = slice(half * HALF, half * HALF + HALF)
                hold(dve, top_found, n + 1)
                nc.vector.tensor_scalar(slot_idx[:, c], top[:, c], -1.0, None, ALU.mult).then_inc(idx_ready, 1)

            load_keys(0, 0)
            dve.wait_ge(keys_loaded, 1)
            find(0)
            hand(0, 0)
            hand(0, 1)
            dve.wait_ge(par_turned, 1)
            nc.vector.tensor_copy(par[:, :], par_ps).then_inc(par_ready, 1)
            dve.wait_ge(alphas_loaded, 48)
            nc.vector.tensor_scalar(rest[:, :], alphas[:, :], -1.0, 1.0, ALU.mult, ALU.add).then_inc(par_ready, 1)
            dve.wait_ge(last_loaded, 16)
            dve.wait_ge(users_landed, 16 * TILES)

            def score_half(g, half):
                for j in range(half * HALF, half * HALF + HALF):
                    dve.wait_ge(landed[j], 16 * (g + 1))
                    nc.vector.tensor_tensor_reduce(prod[:, j, :], rows[:, j, :], user_now, 1.0, 0.0,
                                                   ALU.mult, ALU.add, score[:, j:j + 1]).then_inc(scored, 1)

            def layer1_stats(t):
                hold(dve, l1_kept, M1 * (t + 1))
                for m in range(M1):
                    nc.vector.bn_stats(stats1[:, m, t, :], h1[:, m, bass.ds(t * P, P)]).then_inc(stats_done, 1)

            def tile(t, lag):
                first, end = span(dve, t)
                if lag:
                    hold(dve, scored, GROUP * first)
                nc.vector.tensor_copy(user_now, user_rows[:, t, :]).then_inc(user_set, 1)
                hold(dve, user_set, t + 1)
                nc.vector.tensor_tensor_reduce(last_prod[:, :], last_row[:, :], user_now, 1.0, 0.0,
                                               ALU.mult, ALU.add, last_score[:, :]).then_inc(last_dotted, 1)
                hold(dve, last_dotted, t + 1)
                nc.vector.tensor_scalar(last_weight[:, :], last_score[:, :], left[:, bass.ds(t, 1)], None,
                                        ALU.mult).then_inc(last_weighed, 1)
                with dve.Fori(first, end - 1) as g:
                    score_half(g, 0)
                    find(g + 1)
                    hand(g + 1, 0)
                    score_half(g, 1)
                    hand(g + 1, 1)
                score_half(end - 1, 0)
                load_keys(t + 1, end)
                hold(dve, keys_loaded, t + 2)
                find(end)
                hand(end, 0)
                score_half(end - 1, 1)
                hand(end, 1)
                if lag == 2:
                    layer1_stats(t - 2)

            over_tiles(dve, tile)
            layer1_stats(TILES - 2)
            layer1_stats(TILES - 1)

            for n, (m, src, stats, spans, g_c, be_c, F) in enumerate((
                    (M1, h1, stats1, TILES, g1c, be1c, D1), (M2, h2, stats2, CHUNKS, g2c, be2c, D2))):
                dve.wait_ge((stats_done, l2_stats_done)[n], m * spans)
                for k in range(m):
                    nc.vector.bn_aggr(mv[:, k, :], stats[:, k, :, :].rearrange("p t s -> p (t s)")).then_inc(bn_step[n], 1)
                dve.wait_ge(bn_step[n], m)
                nc.vector.tensor_scalar(bn_v[:, 0:m], mv[:, 0:m, 1], BN_EPS, None, ALU.add).then_inc(aggregated[n], 1)
                dve.wait_ge(bn_rooted[n], 1)
                nc.vector.reciprocal(bn_r[:, 0:m], bn_s[:, 0:m]).then_inc(bn_step[n], 1)
                dve.wait_ge(bn_step[n], m + 1)
                nc.vector.tensor_tensor(scale[n][:, 0:m], bn_r[:, 0:m], g_c, ALU.mult).then_inc(bn_step[n], 1)
                dve.wait_ge(bn_step[n], m + 2)
                nc.vector.tensor_tensor(bn_m[:, 0:m], mv[:, 0:m, 0], scale[n][:, 0:m], ALU.mult).then_inc(bn_step[n], 1)
                dve.wait_ge(bn_step[n], m + 3)
                nc.vector.tensor_tensor(shift[n][:, 0:m], be_c, bn_m[:, 0:m], ALU.subtract).then_inc(bn_ready[n], 1)

                def step(i, odd, live):
                    d_i, d_p = (dev[x][:, 0:m * CHUNK].rearrange("p (m b) -> p m b", m=m) for x in (odd, 1 - odd))
                    if live(0):
                        hold(dve, normed_act[n], m // 2 * (i + 1))
                        hold(dve, normed_pool[n], m // 2 * (i + 1))
                        hold(dve, avg_ready[n], i)
                        nc.vector.tensor_reduce(col_sum[:, :], src[:, 0:m, chunk(i)].rearrange("p m b -> p b m"),
                                                AX_X, ALU.add).then_inc(col_summed[n], 1)
                    if live(1):
                        hold(dve, squared[n], i)
                        nc.vector.tensor_reduce(sq_sum[:, :], dev_sq[:, 0:m * CHUNK].rearrange("p (m b) -> p b m", m=m),
                                                AX_X, ALU.add).then_inc(sq_summed[n], 1)
                    if live(2):
                        dve.wait_ge(mixed[n], i - 1)
                        nc.vector.tensor_tensor(src[:, 0:m, chunk(i - 2)], d_i, src[:, 0:m, chunk(i - 2)],
                                                ALU.mult).then_inc(dice_done[n], 1)
                    if live(1):
                        hold(dve, var_ready[n], i)
                        nc.vector.tensor_scalar(var_eps[:, :], var_ps, F * DICE_EPS, None, ALU.add).then_inc(var_kept[n], 1)
                    if live(0):
                        hold(dve, avg_ready[n], i + 1)
                        if live(2):
                            hold(dve, dice_done[n], i - 1)
                        nc.vector.tensor_tensor(d_i, src[:, 0:m, chunk(i)],
                                                avg_ps.unsqueeze(1).to_broadcast([P, m, CHUNK]),
                                                ALU.subtract).then_inc(dev_ready[n], 1)
                    if live(1):
                        hold(dve, rooted[n], i)
                        nc.vector.reciprocal(inv[:, :], root[:, :]).then_inc(inverted[n], 1)
                        hold(dve, inverted[n], i)
                        nc.vector.tensor_tensor(d_p, d_p, inv[:, :].unsqueeze(1).to_broadcast([P, m, CHUNK]),
                                                ALU.mult).then_inc(arg_ready[n], 1)
                    if n == 0 and live(4):
                        hold(dve, l2_kept, M2 * (i - 3))
                        for k in range(M2):
                            nc.vector.bn_stats(stats2[:, k, i - 4, :], h2[:, k, chunk(i - 4)]).then_inc(l2_stats_done, 1)
                pipelined(dve, step)

        @block.scalar
        def _(act):
            for i in range(2 * TILES // 4):
                act.wait_ge(block_turned, i + 1)
                dst = user_T if i < TILES // 4 else item_T
                k = i % (TILES // 4)
                nc.scalar.activation(dst[:, k * 4 * P:(k + 1) * 4 * P], turn_ps[i % 2], ACT.Copy).then_inc(block_kept, 1)
            act.wait_ge(last_loaded, 16)
            act.wait_ge(par_ready, 2)
            act.wait_ge(plan_ready, 1)
            act.sem_inc(slot_scaled, GROUP)

            def keep_layer1(t):
                hold(act, l1_done, t + 1)
                for m in range(M1):
                    nc.scalar.activation(h1[:, m, bass.ds(t * P, P)], l1_ps[:, m, :], ACT.Identity,
                                         bias=b1c[:, m:m + 1]).then_inc(l1_kept, 1)

            def tile(t, lag):
                first, end = span(act, t)
                hold(act, last_weighed, t + 1)
                hold(act, pooled, t)
                nc.scalar.activation(last_scaled[:, :], last_row[:, :], ACT.Copy,
                                     scale=last_weight[:, 0:1]).then_inc(last_ready, 1)
                with act.Fori(first, end) as g:
                    for j in range(GROUP):
                        act.wait_ge(slot_summed, GROUP * g + j + 1)
                        act.wait_ge(scored, GROUP * g + j + 1)
                        nc.scalar.activation(scaled[:, j, :], rows[:, j, :], ACT.Copy,
                                             scale=score[:, j:j + 1]).then_inc(slot_scaled, 1)
                act.wait_ge(pooled, t + 1)
                nc.scalar.activation(pooled_T[:, :], pooled_ps, ACT.Copy).then_inc(pooled_kept, 1)
                if lag:
                    keep_layer1(t - 1)

            over_tiles(act, tile)
            keep_layer1(TILES - 1)

            for n, (m, src) in enumerate(((M1, h1), (M2, h2))):
                act.wait_ge(aggregated[n], 1)
                nc.scalar.activation(bn_s[:, 0:m], bn_v[:, 0:m], ACT.Sqrt).then_inc(bn_rooted[n], 1)
                act.wait_ge(bn_ready[n], 1)

                def normalise(c):
                    for k in range(m // 2):
                        nc.scalar.activation(src[:, k, chunk(c)], src[:, k, chunk(c)], ACT.Identity,
                                             bias=shift[n][:, k:k + 1], scale=scale[n][:, k:k + 1]).then_inc(normed_act[n], 1)

                normalise(0)
                normalise(1)

                def step(i, odd, live):
                    d_i, d_p = (dev[x][:, 0:m * CHUNK] for x in (odd, 1 - odd))
                    if live(1):
                        hold(act, inverted[n], i - 1)
                        act.wait_ge(var_kept[n], i)
                        nc.scalar.activation(root[:, :], var_eps[:, :], ACT.Sqrt).then_inc(rooted[n], 1)
                    if live(0):
                        hold(act, sq_summed[n], i)
                        act.wait_ge(dev_ready[n], i + 1)
                        nc.scalar.activation(dev_sq[:, 0:m * CHUNK], d_i, ACT.Square).then_inc(squared[n], 1)
                    if live(1):
                        act.wait_ge(arg_ready[n], i)
                        nc.scalar.activation(d_p, d_p, ACT.Sigmoid).then_inc(gated[n], 1)
                    if live(-2):
                        normalise(i + 2)
                    if live(3):
                        if n == 0:
                            hold(act, product_done[0], i - 2)
                            for k in range(M2):
                                nc.scalar.activation(h2[:, k, chunk(i - 3)], l2_ps[1 - odd][:, k, :], ACT.Identity,
                                                     bias=b2c[:, k:k + 1]).then_inc(l2_kept, 1)
                        else:
                            hold(act, product_done[1], i - 2)
                            nc.scalar.activation(y_row[:, chunk(i - 3)], y_ps[1 - odd], ACT.Identity,
                                                 bias=bias3[:, 0:1]).then_inc(y_kept, 1)
                pipelined(act, step)

        @block.tensor
        def _(pe):
            pe.wait_ge(consts_made, N_CONSTS)
            pe.wait_ge(ids_float, 1)
            nc.tensor.transpose(ids_ps, ids_f[:, :], ident[0:2 * TILES, 0:2 * TILES]).then_inc(ids_turned, 1)
            pe.wait_ge(counts_ready, 1)
            nc.tensor.transpose(counts_ps, counts[:, :], ident[:, :]).then_inc(counts_turned, 1)
            pe.wait_ge(fullest_ready, 1)
            nc.tensor.matmul(fullest_ps, fullest_row[:, :], ident[0:TILES, 0:TILES], start=True, stop=True).then_inc(fullest_spread, 1)
            pe.wait_ge(par_loaded, 16 * 7)
            nc.tensor.transpose(par_ps, par_rows[:, :], ident[0:n_par, 0:n_par]).then_inc(par_turned, 1)
            for i in range(2 * TILES // 4):
                if i == 0:
                    pe.wait_ge(users_landed, 16 * TILES)
                if i == TILES // 4:
                    pe.wait_ge(items_landed, 16 * TILES)
                if i >= 2:
                    pe.wait_ge(block_kept, i - 1)
                src = user_rows if i < TILES // 4 else item_rows
                for k in range(4):
                    mm = nc.tensor.transpose(turn_ps[i % 2][:, k * P:(k + 1) * P], src[:, 4 * (i % (TILES // 4)) + k, :], ident[:, :])
                mm.then_inc(block_turned, 1)
            pe.wait_ge(block_kept, 2 * TILES // 4)
            pe.wait_ge(w1_loaded, 16)
            pe.wait_ge(plan_ready, 1)
            pe.sem_inc(slot_summed, GROUP)

            def layer1(t, again):
                hold(pe, pooled_kept, t + 1)
                if again:
                    hold(pe, l1_kept, M1 * t)
                x = (item_T[:, bass.ds(t * P, P)], pooled_T[:, :], user_T[:, bass.ds(t * P, P)])
                for m in range(M1):
                    for k in range(KX):
                        mm = nc.tensor.matmul(l1_ps[:, m, :], w1[:, k, m * P:(m + 1) * P], x[k],
                                              start=(k == 0), stop=(k == KX - 1))
                mm.then_inc(l1_done, 1)

            def sum_group(g):
                for j in range(GROUP):
                    pe.wait_ge(slot_scaled, GROUP * g + j + 1 + GROUP)
                    nc.tensor.matmul(pooled_ps, scaled[:, j, :], ident[:, :], start=False, stop=False,
                                     skip_group_check=True).then_inc(slot_summed, 1)

            def tile(t, lag):
                first, end = span(pe, t)
                hold(pe, last_ready, t + 1)
                if lag:
                    hold(pe, pooled_kept, t)
                nc.tensor.matmul(pooled_ps, last_scaled[:, :], ident[:, :], start=True, stop=False,
                                 skip_group_check=True)
                if lag:
                    sum_group(first)
                    layer1(t - 1, lag == 2)
                    with pe.Fori(first + 1, end) as g:
                        sum_group(g)
                else:
                    with pe.Fori(first, end) as g:
                        sum_group(g)
                hold(pe, slot_summed, GROUP * end + GROUP)
                pe.sem_inc(pooled, 1)

            over_tiles(pe, tile)
            layer1(TILES - 1, True)
            pe.wait_ge(w2_loaded, 16)

            for n, (m, mean_of) in enumerate(((M1, mean_of1), (M2, mean_of2))):
                if n == 0:
                    pe.wait_ge(l1_kept, M1 * TILES)

                def step(i, odd, live):
                    if live(0):
                        if live(1):
                            hold(pe, dev_ready[n], i)
                        hold(pe, col_summed[n], i + 1)
                        nc.tensor.matmul(avg_ps, mean_of[:, :], col_sum[:, :], start=True, stop=True).then_inc(avg_ready[n], 1)
                    if live(1):
                        hold(pe, var_kept[n], i - 1)
                        hold(pe, sq_summed[n], i)
                        nc.tensor.matmul(var_ps, ones[:, :], sq_sum[:, :], start=True, stop=True).then_inc(var_ready[n], 1)
                    if live(2):
                        hold(pe, dice_done[n], i - 1)
                        if n == 0:
                            if live(4):
                                hold(pe, l2_kept, M2 * (i - 3))
                            for o in range(M2):
                                for k in range(M1):
                                    mm = nc.tensor.matmul(l2_ps[odd][:, o, :], w2[:, k, o * P:(o + 1) * P],
                                                          h1[:, k, chunk(i - 2)], start=(k == 0), stop=(k == M1 - 1))
                        else:
                            if live(4):
                                hold(pe, y_kept, i - 3)
                            for k in range(M2):
                                mm = nc.tensor.matmul(y_ps[odd], w3c[:, k:k + 1], h2[:, k, chunk(i - 2)],
                                                      start=(k == 0), stop=(k == M2 - 1))
                        mm.then_inc(product_done[n], 1)
                pipelined(pe, step)


_INS = ['r_items', 'r_users', 'r_history_users', 'L0_rec_item_table', 'L0_rec_user_table', 'L0_rec_W1', 'L0_rec_b1',
        'L0_rec_g1', 'L0_rec_be1', 'L0_rec_a1', 'L0_rec_W2', 'L0_rec_b2', 'L0_rec_g2', 'L0_rec_be2', 'L0_rec_a2',
        'L0_rec_W3', 'L0_rec_b3']
_OUTS = [((2048, 1), 'float32')]


def kernel(**inputs):
    import numpy as _np
    import concourse.bacc as _bacc
    from concourse import mybir as _mybir
    from concourse.bass_utils import run_bass_kernel_spmd as _run

    nc = _bacc.Bacc("TRN2", target_bir_lowering=False, num_devices=1)
    arrays, args = {}, []
    for name in _INS:
        a = _np.ascontiguousarray(inputs[name])
        arrays[f"in_{name}_dram"] = a
        args.append(nc.dram_tensor(f"in_{name}_dram", a.shape, _mybir.dt.from_np(a.dtype), kind="ExternalInput").ap())
    for i, (shape, dtype) in enumerate(_OUTS):
        dt = _mybir.dt.from_np(_np.dtype(dtype))
        args.append(nc.dram_tensor(f"out_{i}_dram", shape, dt, kind="ExternalOutput").ap())
    recommender_kernel(nc, *args)
    r = _run(nc, [arrays], core_ids=[0])
    got = tuple(r.results[0][f"out_{i}_dram"] for i in range(len(_OUTS)))
    return got[0]
```
